# Optimizing a Trainium2 kernel written in Bass

```python
import numpy as np
import jax
import jax.numpy as jnp

def _softmax(x, axis=-1):
    return jax.nn.softmax(x, axis=axis)

def _gelu(x):
    return jax.nn.gelu(x, approximate=True)

def _silu(x):
    return jax.nn.silu(x)

def _sigmoid(x):
    return jax.nn.sigmoid(x)

def _layernorm(x, axis=-1, eps=1e-05):
    m = jnp.mean(x, axis=axis, keepdims=True)
    v = jnp.var(x, axis=axis, keepdims=True)
    return (x - m) / jnp.sqrt(v + eps)

def _scatter_add(tgt, idx, src, axis=0):
    return tgt.at[idx].add(src)

def _segment_sum(src, seg, n):
    return jax.ops.segment_sum(src, seg, n)
kernel_name = 'mk_cond_resid_d2_seqx_r8_4ebedf'

def setup_inputs(seed: int=0):
    np.random.seed(seed)
    _w = jnp.asarray

    def _rec_inputs():
        import jax
        import jax.numpy as jnp
        _rk = jax.random.key(seed)
        x = 7.22e-05 + 1 * jax.random.normal(jax.random.fold_in(_rk, 1), (64, 32, 512), jnp.float32)
        _lenS = 32 - jax.random.randint(jax.random.fold_in(_rk, 7), (64,), 0, max(1, 32 // 4) + 1, jnp.int32)
        _lenS2 = 32 - jax.random.randint(jax.random.fold_in(_rk, 8), (64,), 0, max(1, 32 // 4) + 1, jnp.int32)
        itok_B_2_6 = jax.random.randint(jax.random.fold_in(_rk, 11), (64,), 2, 7, jnp.int32)
        itok_B_0_15 = jax.random.randint(jax.random.fold_in(_rk, 12), (64,), 0, 16, jnp.int32)
        return (x, itok_B_2_6, itok_B_0_15)
    x, itok_B_2_6, itok_B_0_15 = _rec_inputs()

    def _L0_cond_setup():
        import jax, jax.numpy as jnp
        import numpy as np
        B, N, H, F = (4, 64, 512, 1376)
        L, R, RANK = (1, 16, 16)
        SCALE = 0.5
        key = jax.random.key(seed)
        ks = jax.random.split(key, 12)
        nrm = lambda k, shape, fan: jax.random.normal(k, shape, jnp.float32) * fan ** (-0.5)
        inp = {'x': jax.random.normal(ks[0], (B, N, H), jnp.float32), 'W_gate': nrm(ks[1], (F, H), H), 'W_up': nrm(ks[2], (F, H), H), 'W_down': nrm(ks[3], (H, F), F), 'A_gate': nrm(ks[4], (L, R, RANK, H), H), 'B_gate': nrm(ks[5], (L, R, F, RANK), RANK), 'A_up': nrm(ks[6], (L, R, RANK, H), H), 'B_up': nrm(ks[7], (L, R, F, RANK), RANK), 'A_down': nrm(ks[8], (L, R, RANK, F), F), 'B_down': nrm(ks[9], (L, R, H, RANK), RANK), 'lora_indices': jax.random.randint(ks[10], (B,), 0, R), 'layer_idx': 0}
        return inp
    _L0_cond_all = _L0_cond_setup()
    _L0_cond_in = {k: v for k, v in _L0_cond_all.items() if k in ('W_gate', 'W_up', 'W_down', 'A_gate', 'B_gate', 'A_up', 'B_up', 'A_down', 'B_down')}
    del _L0_cond_all

    def _L1_cond_setup():
        import jax, jax.numpy as jnp
        import numpy as np
        B, C, T = (64, 32, 512)
        S, D = (16, 32)
        key = jax.random.key(seed)
        k1, k2, k3 = jax.random.split(key, 3)
        x = jax.random.normal(k1, (B, C, T), dtype=jnp.float32)
        condition = jax.random.randint(k2, (B,), 0, S, dtype=jnp.int64)
        bound = float(np.sqrt(6.0 / C))
        weights = jax.random.uniform(k3, (S, C, D), dtype=jnp.float32, minval=-bound, maxval=bound)
        return {'x': x, 'condition': condition, 'weights': weights}
    _L1_cond_all = _L1_cond_setup()
    _L1_cond_in = {k: v for k, v in _L1_cond_all.items() if k in ('weights',)}
    del _L1_cond_all
    return {'x': x, 'itok_B_2_6': itok_B_2_6, 'itok_B_0_15': itok_B_0_15, 'L0_cond_W_gate': _L0_cond_in['W_gate'], 'L0_cond_W_up': _L0_cond_in['W_up'], 'L0_cond_W_down': _L0_cond_in['W_down'], 'L0_cond_A_gate': _L0_cond_in['A_gate'], 'L0_cond_B_gate': _L0_cond_in['B_gate'], 'L0_cond_A_up': _L0_cond_in['A_up'], 'L0_cond_B_up': _L0_cond_in['B_up'], 'L0_cond_A_down': _L0_cond_in['A_down'], 'L0_cond_B_down': _L0_cond_in['B_down'], 'L1_cond_weights': _L1_cond_in['weights']}

def reference(x, itok_B_2_6, itok_B_0_15, L0_cond_W_gate, L0_cond_W_up, L0_cond_W_down, L0_cond_A_gate, L0_cond_B_gate, L0_cond_A_up, L0_cond_B_up, L0_cond_A_down, L0_cond_B_down, L1_cond_weights):
    import jax
    import jax.numpy as jnp

    def _L0_cond_ref(x, W_gate, W_up, W_down, A_gate, B_gate, A_up, B_up, A_down, B_down, lora_indices, layer_idx):
        import jax, jax.numpy as jnp
        import numpy as np
        B, N, H, F = (4, 64, 512, 1376)
        L, R, RANK = (1, 16, 16)
        SCALE = 0.5

        def lora_add(base, inp, A, B):
            Ab = A[layer_idx][lora_indices]
            Bb = B[layer_idx][lora_indices]
            t = jnp.einsum('bri,bni->bnr', Ab, inp)
            return base + jnp.einsum('bor,bnr->bno', Bb, t) * SCALE
        gate = lora_add(jnp.einsum('bnh,fh->bnf', x, W_gate), x, A_gate, B_gate)
        up = lora_add(jnp.einsum('bnh,fh->bnf', x, W_up), x, A_up, B_up)
        act = jax.nn.silu(gate) * up
        down = lora_add(jnp.einsum('bnf,hf->bnh', act, W_down), act, A_down, B_down)
        return down

    def _L1_cond_ref(x, condition, weights):
        import jax, jax.numpy as jnp
        import numpy as np
        B, C, T = (64, 32, 512)
        S, D = (16, 32)
        W = weights[condition]
        return jnp.einsum('bct,bcd->bdt', x, W)
    x = x + _L0_cond_ref(x, L0_cond_W_gate, L0_cond_W_up, L0_cond_W_down, L0_cond_A_gate, L0_cond_B_gate, L0_cond_A_up, L0_cond_B_up, L0_cond_A_down, L0_cond_B_down, itok_B_2_6, 0)
    x = x + _L1_cond_ref(x, itok_B_0_15, L1_cond_weights)
    return x

_drawn_inputs = setup_inputs


def setup_inputs(seed=0):
    import zlib

    import numpy as np

    out = dict(_drawn_inputs(seed))
    spreads = {}
    factors = {}
    for name, (base, spread) in spreads.items():
        noise = np.random.default_rng([zlib.crc32(name.encode()), seed]).standard_normal(out[name].shape)
        drawn = base * np.exp(spread * noise) if base else spread * noise
        out[name] = jnp.asarray(drawn.astype(out[name].dtype))
    for name, factor in factors.items():
        out[name] = (out[name] * factor).astype(out[name].dtype)
    return out
```

```python
from contextlib import ExitStack

import concourse.bass as bass
from concourse import mybir

F32 = mybir.dt.float32
F32R = mybir.dt.float32r
I32 = mybir.dt.int32
ALU = mybir.AluOpType
ACT = mybir.ActivationFunctionType

P = 128
SEQS, CH, H = 64, 32, 512
F = 1376
ADAPTERS, RANK = 16, 16
LORA_SCALE = 0.5
TILE_SEQS = P // CH
TILES = SEQS // TILE_SEQS
KH = H // P
RR = TILE_SEQS * RANK
SECTIONS = [(0, 512), (512, 512), (1024, F - 1024)]
NS = len(SECTIONS)
CHUNKS = [(c * P, min(P, F - c * P)) for c in range(-(-F // P))]
NC = len(CHUNKS)
A_GU = KH * 2 * RANK
A_ROW = A_GU + NC * RANK
B_ROW = 2 * F + H
WD = H + RR
HALF = WD // 2
PIECE = 1024
SLOTS = 4


def weight_pieces():
    pieces = []
    for c0, n in SECTIONS:
        for m in ("gate", "up"):
            for half in range(2):
                pieces.append((m, KH * c0 + half * 2 * n, 2 * n))
    for c in range(0, NC, 2):
        if c + 1 < NC and CHUNKS[c + 1][1] == P:
            pieces.append(("down", c, 2))
        else:
            pieces += [("down", i, 1) for i in range(c, min(c + 2, NC))]
    return pieces


PIECES = weight_pieces()
SECTION_PIECES = [4 * (s + 1) for s in range(NS)]


def section_of(chunk):
    return min(chunk // 4, NS - 1)


def build(nc, x, xT, w_gate, w_up, w_down, a_rows, b_rows, mix_rows, which, mult, lane, out):
    with ExitStack() as ctx:
        def sb(name, shape, dt=F32):
            return ctx.enter_context(nc.sbuf_tensor(name, shape, dt))

        def bank(name):
            return ctx.enter_context(nc.psum_tensor(name, [P, 512], F32))

        def sem(name):
            return ctx.enter_context(nc.semaphore(name))

        w_hi = {m: sb(f"w_{m}_hi", [P, KH * F], F32R) for m in ("gate", "up")}
        w_lo = {m: sb(f"w_{m}_lo", [P, KH * F], F32R) for m in ("gate", "up")}
        wd_hi = sb("wd_hi", [P, NC, WD], F32R)
        wd_lo = sb("wd_lo", [P, NC, WD], F32R)
        landing = sb("landing", [P, SLOTS, PIECE])
        a_raw = sb("a_raw", [P, TILE_SEQS, A_ROW])
        a_gu = sb("a_gu", [P, KH, 2, 2 * RR], F32R)
        b_raw = sb("b_raw", [RR, B_ROW])
        b_gu = sb("b_gu", [P, 2 * F], F32R)
        b_dn = sb("b_dn", [P, H], F32R)
        xT_raw = sb("xT_raw", [P, KH * P])
        xT_hi = sb("xT_hi", [P, KH * P], F32R)
        xT_lo = sb("xT_lo", [P, KH * P], F32R)
        x_sb = sb("x_sb", [P, H])
        out_sb = sb("out_sb", [P, H])
        t_mid = sb("t_mid", [P, 2 * RR])
        t_sum = sb("t_sum", [P, 2 * RR])
        t_gu = sb("t_gu", [P, 2, 2 * RR])
        t_dn = sb("t_dn", [P, 2 * RR])
        tT_hi = sb("tT_hi", [P, 2, P], F32R)
        tT_lo = sb("tT_lo", [P, 2, P], F32R)
        tdT_hi = sb("tdT_hi", [P, P], F32R)
        tdT_lo = sb("tdT_lo", [P, P], F32R)
        act = [sb(f"act{i}", [P, 512]) for i in range(2)]
        actT_hi = sb("actT_hi", [P, NC, P], F32R)
        actT_lo = sb("actT_lo", [P, NC, P], F32R)
        mix_raw = sb("mix_raw", [P, CH])
        mix_w = sb("mix_w", [P, P])
        ident = sb("ident", [P, P])
        mask = sb("mask", [P, RR])
        which_sb = sb("which_sb", [P, TILES, TILE_SEQS + 2], I32)
        mult_sb = sb("mult_sb", [P, TILE_SEQS + 2], I32)
        lane_sb = sb("lane_sb", [P, TILE_SEQS + 2], I32)
        scaled = sb("scaled", [P, TILES, TILE_SEQS + 2], I32)
        rows = sb("rows", [P, TILES, TILE_SEQS + 2], I32)
        waited = sb("waited", [1, 1], I32)
        rows_now = sb("rows_now", [P, TILE_SEQS + 1], I32)
        mix_rows_now = sb("mix_rows_now", [P, 1], I32)

        ps_gate = [bank(f"ps_gate{i}") for i in range(2)]
        ps_up = [bank(f"ps_up{i}") for i in range(2)]
        ps_down = [bank(f"ps_down{i}") for i in range(2)]
        ps_turn = bank("ps_turn")
        ps_misc = bank("ps_misc")

        w_landed = [sem(f"w_landed{i}") for i in range(SLOTS)]
        which_landed = sem("which_landed")
        xT_landed = sem("xT_landed")
        x_landed = sem("x_landed")
        a_landed = sem("a_landed")
        b_landed = sem("b_landed")
        mix_landed = sem("mix_landed")
        stored = sem("stored")
        ident_zeroed = sem("ident_zeroed")
        ident_ready = sem("ident_ready")
        mask_zeroed = sem("mask_zeroed")
        mask_ready = sem("mask_ready")
        scaled_ready = sem("scaled_ready")
        rows_ready = sem("rows_ready")
        rows_copied = sem("rows_copied")
        mix_rows_copied = sem("mix_rows_copied")
        w_hi_ready = sem("w_hi_ready")
        xT_hi_ready = sem("xT_hi_ready")
        a_gu_hi_ready = sem("a_gu_hi_ready")
        b_gu_hi_ready = sem("b_gu_hi_ready")
        a_dn_hi_ready = sem("a_dn_hi_ready")
        b_dn_hi_ready = sem("b_dn_hi_ready")
        t_mid_ready = sem("t_mid_ready")
        tT_hi_ready = sem("tT_hi_ready")
        tdT_hi_ready = sem("tdT_hi_ready")
        silu_ready = sem("silu_ready")
        actT_hi_ready = sem("actT_hi_ready")
        w_ready = sem("w_ready")
        xT_ready = sem("xT_ready")
        a_gu_ready = sem("a_gu_ready")
        b_gu_ready = sem("b_gu_ready")
        a_dn_ready = sem("a_dn_ready")
        b_dn_ready = sem("b_dn_ready")
        t_sum_ready = sem("t_sum_ready")
        t_gu_ready = sem("t_gu_ready")
        tT_ready = sem("tT_ready")
        t_dn_ready = sem("t_dn_ready")
        tdT_ready = sem("tdT_ready")
        act_ready = sem("act_ready")
        actT_ready = sem("actT_ready")
        mix_ready = sem("mix_ready")
        h_ready = sem("h_ready")
        out_ready = sem("out_ready")
        t_done = sem("t_done")
        xT_used = sem("xT_used")
        section_done = sem("section_done")
        t_turned = sem("t_turned")
        td_turned = sem("td_turned")
        act_turned = sem("act_turned")
        down_done = sem("down_done")
        down_lora_done = sem("down_lora_done")
        mix_done = sem("mix_done")

        def w_at(w, s, k):
            c0, n = SECTIONS[s]
            return w[:, KH * c0 + k * n:KH * c0 + (k + 1) * n]

        block = ctx.enter_context(nc.Block())

        @block.sync
        def _(sp):
            def load_xT(t):
                sp.dma_start(xT_raw[:, :], xT[bass.ds(t * P, P), :]).then_inc(xT_landed, 16)

            def load_x(t):
                sp.dma_start(x_sb[:, :], x[bass.ds(t * P, P), :]).then_inc(x_landed, 16)

            def store(t):
                sp.wait_ge(out_ready, t + 1)
                sp.dma_start(out[bass.ds(t * P, P), :], out_sb[:, :]).then_inc(stored, 16)

            sp.dma_start(which_sb[:, :, :], which).then_inc(which_landed, 16)
            sp.dma_start(mult_sb[:, :], mult).then_inc(which_landed, 16)
            sp.dma_start(lane_sb[:, :], lane).then_inc(which_landed, 16)
            load_xT(0)
            for n, (m, at, cols) in enumerate(PIECES):
                if n == SECTION_PIECES[2]:
                    sp.wait_ge(xT_ready, 1)
                    load_xT(1)
                    load_x(0)
                if n >= SLOTS:
                    sp.wait_ge(w_ready, n - SLOTS + 1)
                slot = landing[:, n % SLOTS, :]
                if m == "down":
                    k = CHUNKS[at][1]
                    sp.dma_start(slot[0:k, 0:cols * H].rearrange("p (c n) -> p c n", n=H),
                                 w_down[at * P:at * P + cols * k, :].rearrange("(c p) n -> p c n", p=k))\
                      .then_inc(w_landed[n % SLOTS], 16)
                else:
                    src = w_gate if m == "gate" else w_up
                    sp.dma_start(slot[:, 0:cols], src[:, at:at + cols]).then_inc(w_landed[n % SLOTS], 16)
            with sp.Fori(2, TILES) as t:
                sp.wait_ge(xT_ready, t)
                load_xT(t)
                store(t - 2)
                load_x(t - 1)
            for t in (TILES - 2, TILES - 1):
                store(t)
                if t + 1 < TILES:
                    load_x(t + 1)
            sp.wait_ge(stored, 16 * TILES)

        @block.gpsimd
        def _(pool):
            pool.memset(ident[:, :], 0.0).then_inc(ident_zeroed, 1)
            pool.wait_ge(ident_zeroed, 1)
            pool.affine_select(out=ident[:, :], in_=ident[:, :], compare_op=ALU.not_equal, fill=1.0, base=0,
                               pattern=[[-1, P]], channel_multiplier=1).then_inc(ident_ready, 1)
            pool.wait_ge(rows_ready, 1)

            def indirect_after(semaphore, value):
                pool.wait_ge(semaphore, value)
                pool.tensor_tensor(waited[:, :], lane_sb[0:1, 0:1], lane_sb[0:1, 0:1], ALU.add)

            def gathers(t, first=False):
                if not first:
                    pool.wait_ge(a_dn_ready, t)
                    pool.wait_ge(b_dn_ready, t)
                now = rows[:, bass.ds(t, 1), :].rearrange("p o c -> p (o c)")
                pool.tensor_copy(rows_now[:, :], now[:, 0:TILE_SEQS + 1])\
                    .then_inc(rows_copied, 1)
                indirect_after(rows_copied, t + 1)
                for q in range(TILE_SEQS):
                    pool.indirect_dma_start(
                        a_raw[:, q, :], None, a_rows,
                        bass.IndirectOffsetOnAxis(ap=rows_now[:, q:q + 1], axis=0)).then_inc(a_landed, 16)
                pool.indirect_dma_start(
                    b_raw[:, :], None, b_rows,
                    bass.IndirectOffsetOnAxis(ap=rows_now[0:RR, TILE_SEQS:TILE_SEQS + 1], axis=0))\
                    .then_inc(b_landed, 16)
                if not first:
                    pool.wait_ge(mix_ready, t)
                pool.tensor_copy(mix_rows_now[:, :], now[:, TILE_SEQS + 1:TILE_SEQS + 2]).then_inc(mix_rows_copied, 1)
                indirect_after(mix_rows_copied, t + 1)
                pool.indirect_dma_start(
                    mix_raw[:, :], None, mix_rows,
                    bass.IndirectOffsetOnAxis(ap=mix_rows_now[:, :], axis=0))\
                    .then_inc(mix_landed, 16)

            gathers(0, first=True)
            with pool.Fori(1, TILES) as t:
                gathers(t)

        @block.scalar
        def _(sc):
            def hi(dst, src):
                return nc.scalar.activation(dst, src, ACT.Copy)

            def split_x(t, first=False):
                sc.wait_ge(xT_landed, 16 * (t + 1))
                if not first:
                    sc.wait_ge(xT_used, t)
                hi(xT_hi[:, :], xT_raw[:, :]).then_inc(xT_hi_ready, 1)

            def split_a_gu(t, first=False):
                sc.wait_ge(a_landed, 16 * TILE_SEQS * (t + 1))
                if not first:
                    sc.wait_ge(t_done, t)
                hi(a_gu[:, :, 0, :].rearrange("p k (q c) -> p q k c", q=TILE_SEQS),
                   a_raw[:, :, 0:A_GU].rearrange("p q (k c) -> p q k c", k=KH)).then_inc(a_gu_hi_ready, 1)

            def split_b_gu(t, first=False):
                sc.wait_ge(b_landed, 16 * (t + 1))
                if not first:
                    sc.wait_ge(section_done, NS * t)
                hi(b_gu[0:RR, :], b_raw[:, 0:2 * F]).then_inc(b_gu_hi_ready, 1)

            def split_weights(n0, n1):
                for n in range(n0, n1):
                    m, at, cols = PIECES[n]
                    sc.wait_ge(w_landed[n % SLOTS], 16 * (n // SLOTS + 1))
                    slot = landing[:, n % SLOTS, :]
                    if m == "down":
                        k = CHUNKS[at][1]
                        hi(wd_hi[0:k, at:at + cols, 0:H],
                           slot[0:k, 0:cols * H].rearrange("p (c n) -> p c n", n=H)).then_inc(w_hi_ready, 1)
                    else:
                        hi(w_hi[m][:, at:at + cols], slot[:, 0:cols]).then_inc(w_hi_ready, 1)

            def turn_td(t):
                sc.wait_ge(td_turned, t + 1)
                hi(tdT_hi[:, :], ps_turn[:, 0:P]).then_inc(tdT_hi_ready, 1)

            def silu(t, s):
                n = SECTIONS[s][1]
                sc.wait_ge(section_done, NS * t + s + 1)
                if s == 2:
                    sc.wait_ge(act_turned, NS * t + 1)
                nc.scalar.activation(act[s % 2][:, 0:n], ps_gate[s % 2][:, 0:n], ACT.Silu).then_inc(silu_ready, 1)

            def act_hi(t, s):
                sc.wait_ge(act_turned, NS * t + s + 1)
                for c in range(4 * s, min(4 * s + 4, NC)):
                    if CHUNKS[c][1] < P:
                        continue
                    last = c
                c0, m = 4 * s, last + 1 - 4 * s
                i = hi(actT_hi[:, c0:c0 + m, :], ps_turn[:, 0:m * P].rearrange("p (c n) -> p c n", n=P))
                if s == NS - 1:
                    k = CHUNKS[-1][1]
                    i = hi(actT_hi[0:k, NC - 1, :], ps_turn[0:k, m * P:(m + 1) * P])
                i.then_inc(actT_hi_ready, 1)

            def adapters_down(t, first):
                hi(wd_hi[:, :, H:WD].rearrange("p c (q r) -> p q c r", q=TILE_SEQS),
                   a_raw[:, :, A_GU:A_ROW].rearrange("p q (c r) -> p q c r", c=NC)).then_inc(a_dn_hi_ready, 1)
                if not first:
                    sc.wait_ge(down_lora_done, t)
                hi(b_dn[0:RR, :], b_raw[:, 2 * F:B_ROW]).then_inc(b_dn_hi_ready, 1)

            def tile(t, first=False, last=False):
                if first:
                    split_x(t, first)
                    split_weights(0, 2)
                    split_a_gu(t, first)
                    split_weights(2, 6)
                else:
                    turn_td(t - 1)
                sc.wait_ge(t_done, t + 1)
                hi(t_mid[:, :], ps_misc[:, 2 * RR:4 * RR]).then_inc(t_mid_ready, 1)
                if first:
                    split_b_gu(t, first)
                sc.wait_ge(t_turned, t + 1)
                hi(tT_hi[:, :, :], ps_turn[:, 0:2 * P].rearrange("p (g n) -> p g n", g=2)).then_inc(tT_hi_ready, 1)
                if first:
                    split_weights(6, 8)
                else:
                    adapters_down(t, first)
                silu(t, 0)
                if first:
                    split_weights(8, 10)
                act_hi(t, 0)
                if first:
                    split_weights(10, 12)
                    adapters_down(t, first)
                silu(t, 1)
                if first:
                    split_weights(12, 14)
                act_hi(t, 1)
                if not last:
                    split_x(t + 1)
                if first:
                    split_weights(14, 16)
                silu(t, 2)
                if first:
                    split_weights(16, len(PIECES))
                act_hi(t, 2)
                if not last:
                    split_a_gu(t + 1)
                    split_b_gu(t + 1)

            tile(0, first=True)
            with sc.Fori(1, TILES - 1) as t:
                tile(t)
            tile(TILES - 1, last=True)
            turn_td(TILES - 1)

        @block.vector
        def _(ve):
            def lo(dst, src, hi_part):
                return nc.vector.tensor_tensor(dst, src, hi_part.bitcast(F32), ALU.subtract)

            def split_x(t):
                ve.wait_ge(xT_hi_ready, t + 1)
                lo(xT_lo[:, :], xT_raw[:, :], xT_hi[:, :]).then_inc(xT_ready, 1)

            def split_a_gu(t):
                ve.wait_ge(a_gu_hi_ready, t + 1)
                lo(a_gu[:, :, 1, :].rearrange("p k (q c) -> p q k c", q=TILE_SEQS),
                   a_raw[:, :, 0:A_GU].rearrange("p q (k c) -> p q k c", k=KH),
                   a_gu[:, :, 0, :].rearrange("p k (q c) -> p q k c", q=TILE_SEQS)).then_inc(a_gu_ready, 1)

            def split_b_gu(t):
                ve.wait_ge(b_gu_hi_ready, t + 1)
                lo(b_gu[RR:2 * RR, :], b_raw[:, 0:2 * F], b_gu[0:RR, :]).then_inc(b_gu_ready, 1)

            def split_weights(n0, n1):
                for n in range(n0, n1):
                    m, at, cols = PIECES[n]
                    ve.wait_ge(w_hi_ready, n + 1)
                    slot = landing[:, n % SLOTS, :]
                    if m == "down":
                        k = CHUNKS[at][1]
                        lo(wd_lo[0:k, at:at + cols, 0:H], slot[0:k, 0:cols * H].rearrange("p (c n) -> p c n", n=H),
                           wd_hi[0:k, at:at + cols, 0:H]).then_inc(w_ready, 1)
                    else:
                        lo(w_lo[m][:, at:at + cols], slot[:, 0:cols], w_hi[m][:, at:at + cols]).then_inc(w_ready, 1)

            def twice(ap, lead):
                o = ap.rearrange("p (o q r) -> p o q r", o=1, q=TILE_SEQS) if lead is None else lead
                return o.to_broadcast([P, 2, TILE_SEQS, RANK])

            mask2 = twice(mask[:, :], None)

            def mask_td(t):
                ve.wait_ge(down_done, t + 1)
                nc.vector.tensor_tensor(
                    t_dn[:, :].rearrange("p (o q r) -> p o q r", o=2, q=TILE_SEQS),
                    twice(ps_down[1][:, HALF - RR:HALF], None), mask2, ALU.mult).then_inc(t_dn_ready, 1)

            def mask_t(t):
                ve.wait_ge(t_mid_ready, t + 1)
                nc.vector.tensor_tensor(t_sum[:, :], ps_misc[:, 0:2 * RR], t_mid[:, :], ALU.add)\
                    .then_inc(t_sum_ready, 1)
                ve.wait_ge(t_sum_ready, t + 1)
                by_seq = t_sum[:, :].rearrange("p (o q g r) -> p o q g r", o=1, q=TILE_SEQS, g=2)
                for g in range(2):
                    last = nc.vector.tensor_tensor(
                        t_gu[:, g, :].rearrange("p (o q r) -> p o q r", o=2, q=TILE_SEQS),
                        twice(None, by_seq[:, :, :, g, :]), mask2, ALU.mult)
                last.then_inc(t_gu_ready, 1)

            def turn_td(t):
                ve.wait_ge(tdT_hi_ready, t + 1)
                lo(tdT_lo[:, :], ps_turn[:, 0:P], tdT_hi[:, :]).then_inc(tdT_ready, 1)

            def turn_t(t):
                ve.wait_ge(tT_hi_ready, t + 1)
                lo(tT_lo[:, :, :], ps_turn[:, 0:2 * P].rearrange("p (g n) -> p g n", g=2), tT_hi[:, :, :])\
                    .then_inc(tT_ready, 1)

            def spread_mix(t):
                ve.wait_ge(mix_landed, 16 * (t + 1))
                for q in range(TILE_SEQS):
                    r = slice(q * CH, (q + 1) * CH)
                    last = nc.vector.tensor_copy(mix_w[r, r], mix_raw[r, :])
                last.then_inc(mix_ready, 1)

            def residual_h(t):
                ve.wait_ge(x_landed, 16 * (t + 1))
                ve.wait_ge(down_lora_done, t + 1)
                nc.vector.tensor_tensor(x_sb[:, 0:HALF], x_sb[:, 0:HALF], ps_down[0][:, 0:HALF], ALU.add)
                nc.vector.tensor_tensor(x_sb[:, HALF:H], x_sb[:, HALF:H], ps_down[1][:, 0:H - HALF], ALU.add)\
                    .then_inc(h_ready, 1)

            def residual_out(t, first=False):
                ve.wait_ge(mix_done, t + 1)
                if not first:
                    ve.wait_ge(stored, 16 * t)
                nc.vector.tensor_tensor(out_sb[:, :], x_sb[:, :], ps_misc[:, 0:H], ALU.add).then_inc(out_ready, 1)

            def gating(t, s):
                n = SECTIONS[s][1]
                ve.wait_ge(silu_ready, NS * t + s + 1)
                nc.vector.tensor_tensor(act[s % 2][:, 0:n], act[s % 2][:, 0:n], ps_up[s % 2][:, 0:n], ALU.mult)\
                    .then_inc(act_ready, 1)

            def act_lo(t, s):
                ve.wait_ge(actT_hi_ready, NS * t + s + 1)
                c0 = 4 * s
                m = sum(n == P for _, n in CHUNKS[c0:c0 + 4])
                i = lo(actT_lo[:, c0:c0 + m, :], ps_turn[:, 0:m * P].rearrange("p (c n) -> p c n", n=P),
                       actT_hi[:, c0:c0 + m, :])
                if s == NS - 1:
                    k = CHUNKS[-1][1]
                    i = lo(actT_lo[0:k, NC - 1, :], ps_turn[0:k, m * P:(m + 1) * P], actT_hi[0:k, NC - 1, :])
                i.then_inc(actT_ready, 1)

            def adapters_down(t):
                ve.wait_ge(a_dn_hi_ready, t + 1)
                lo(wd_lo[:, :, H:WD].rearrange("p c (q r) -> p q c r", q=TILE_SEQS),
                   a_raw[:, :, A_GU:A_ROW].rearrange("p q (c r) -> p q c r", c=NC),
                   wd_hi[:, :, H:WD].rearrange("p c (q r) -> p q c r", q=TILE_SEQS)).then_inc(a_dn_ready, 1)
                ve.wait_ge(b_dn_hi_ready, t + 1)
                lo(b_dn[RR:2 * RR, :], b_raw[:, 2 * F:B_ROW], b_dn[0:RR, :]).then_inc(b_dn_ready, 1)

            def tile(t, first=False, last=False):
                if first:
                    split_x(t)
                    split_weights(0, 2)
                    split_a_gu(t)
                    split_weights(2, 6)
                else:
                    mask_td(t - 1)
                mask_t(t)
                if first:
                    split_b_gu(t)
                else:
                    turn_td(t - 1)
                turn_t(t)
                if first:
                    split_weights(6, 8)
                else:
                    spread_mix(t - 1)
                    residual_h(t - 1)
                    adapters_down(t)
                gating(t, 0)
                if first:
                    split_weights(8, 10)
                else:
                    residual_out(t - 1, first=isinstance(t, int) and t == 1)
                act_lo(t, 0)
                if first:
                    split_weights(10, 12)
                    adapters_down(t)
                gating(t, 1)
                if first:
                    split_weights(12, 14)
                act_lo(t, 1)
                if not last:
                    split_x(t + 1)
                if first:
                    split_weights(14, 16)
                gating(t, 2)
                if first:
                    split_weights(16, len(PIECES))
                act_lo(t, 2)
                if not last:
                    split_a_gu(t + 1)
                    split_b_gu(t + 1)

            nc.vector.memset(mix_w[:, :], 0.0).then_inc(mask_zeroed, 1)
            nc.vector.memset(mask[:, :], 0.0).then_inc(mask_zeroed, 1)
            ve.wait_ge(mask_zeroed, 2)
            for q in range(TILE_SEQS):
                last = nc.vector.memset(mask[q * CH:(q + 1) * CH, q * RANK:(q + 1) * RANK], LORA_SCALE)
            last.then_inc(mask_ready, 1)
            ve.wait_ge(which_landed, 48)
            each = [P, TILES, TILE_SEQS + 2]
            nc.vector.tensor_tensor(scaled[:, :, :], which_sb[:, :, :],
                                    mult_sb[:, :].rearrange("p (o c) -> p o c", o=1).to_broadcast(each),
                                    ALU.mult).then_inc(scaled_ready, 1)
            ve.wait_ge(scaled_ready, 1)
            nc.vector.tensor_tensor(rows[:, :, :], scaled[:, :, :],
                                    lane_sb[:, :].rearrange("p (o c) -> p o c", o=1).to_broadcast(each),
                                    ALU.add).then_inc(rows_ready, 1)

            ve.wait_ge(mask_ready, 1)
            tile(0, first=True)
            tile(1)
            with ve.Fori(2, TILES - 1) as t:
                tile(t)
            tile(TILES - 1, last=True)
            mask_td(TILES - 1)
            turn_td(TILES - 1)
            spread_mix(TILES - 1)
            residual_h(TILES - 1)
            residual_out(TILES - 1)

        @block.tensor
        def _(pe):
            def base(ps, m, s):
                n = SECTIONS[s][1]
                for k in range(KH):
                    x_hi, x_lo = xT_hi[:, k * P:(k + 1) * P], xT_lo[:, k * P:(k + 1) * P]
                    pe.matmul(ps[:, 0:n], x_hi, w_at(w_hi[m], s, k), start=(k == 0), stop=False)
                    pe.matmul(ps[:, 0:n], x_hi, w_at(w_lo[m], s, k), start=False, stop=False)
                    last = pe.matmul(ps[:, 0:n], x_lo, w_at(w_hi[m], s, k), start=False, stop=False)
                return last

            def lora(ps, g, s):
                c0, n = SECTIONS[s]
                b = b_gu[:, g * F + c0:g * F + c0 + n]
                pe.matmul(ps[:, 0:n], tT_hi[:, g, :], b, start=False, stop=False)
                return pe.matmul(ps[:, 0:n], tT_lo[:, g, :], b, start=False, stop=True)

            def low_rank(t, first=False):
                pe.wait_ge(xT_ready, t + 1)
                pe.wait_ge(a_gu_ready, t + 1)
                if not first:
                    pe.wait_ge(act_ready, NS * t)
                for k in range(KH):
                    x_hi, x_lo = xT_hi[:, k * P:(k + 1) * P], xT_lo[:, k * P:(k + 1) * P]
                    pe.matmul(ps_misc[:, 0:4 * RR], x_hi, a_gu[:, k, :, :].rearrange("p s c -> p (s c)"),
                              start=(k == 0), stop=(k == KH - 1), skip_group_check=True)
                    last = pe.matmul(ps_misc[:, 0:2 * RR], x_lo, a_gu[:, k, 0, :], start=False,
                                     stop=(k == KH - 1), skip_group_check=True)
                last.then_inc(t_done, 1)

            def turn_act(t, s):
                pe.wait_ge(act_ready, NS * t + s + 1)
                if s == 0:
                    pe.wait_ge(tT_ready, t + 1)
                else:
                    pe.wait_ge(actT_ready, NS * t + s)
                for i, (c0, n) in enumerate(CHUNKS[4 * s:4 * s + 4]):
                    at = c0 - SECTIONS[s][0]
                    last = pe.transpose(ps_turn[0:n, i * P:(i + 1) * P], act[s % 2][:, at:at + n], ident[:, :])
                last.then_inc(act_turned, 1)

            def down_chunks(t, c0, c1):
                for c in range(c0, c1):
                    if c == c0 or c % 4 == 0:
                        pe.wait_ge(actT_ready, NS * t + section_of(c) + 1)
                    k = CHUNKS[c][1]
                    for a, w, go in ((actT_hi, wd_hi, c == 0), (actT_hi, wd_lo, False), (actT_lo, wd_hi, False)):
                        for half in range(2):
                            last = pe.matmul(ps_down[half][:, 0:HALF], a[0:k, c, :],
                                             w[0:k, c, half * HALF:(half + 1) * HALF],
                                             start=go, stop=(c == NC - 1 and a is actT_lo))
                return last

            def turn_td(t):
                pe.wait_ge(t_dn_ready, t + 1)
                pe.wait_ge(actT_ready, NS * (t + 1))
                pe.transpose(ps_turn[:, 0:P], t_dn[:, :], ident[:, :]).then_inc(td_turned, 1)

            def down_lora(t):
                pe.wait_ge(tdT_ready, t + 1)
                for td in (tdT_hi, tdT_lo):
                    stop = td is tdT_lo
                    pe.matmul(ps_down[0][:, 0:HALF], td[:, :], b_dn[:, 0:HALF], start=False, stop=stop,
                              skip_group_check=True)
                    last = pe.matmul(ps_down[1][:, 0:H - HALF], td[:, :], b_dn[:, HALF:H], start=False, stop=stop,
                                     skip_group_check=True)
                last.then_inc(down_lora_done, 1)

            def mix(t):
                pe.wait_ge(mix_ready, t + 1)
                pe.wait_ge(h_ready, t + 1)
                pe.matmul(ps_misc[:, 0:H], mix_w[:, :], x_sb[:, :], start=True, stop=True).then_inc(mix_done, 1)

            def tile(t, first=False):
                def weights(pieces):
                    if first:
                        pe.wait_ge(w_ready, pieces)

                if first:
                    pe.wait_ge(xT_ready, 1)
                    weights(2)
                else:
                    low_rank(t)
                base(ps_gate[0], "gate", 0)
                if first:
                    low_rank(t, first)
                    weights(4)
                else:
                    turn_td(t - 1)
                base(ps_up[0], "up", 0)
                pe.wait_ge(t_gu_ready, t + 1)
                if not first:
                    pe.wait_ge(tdT_ready, t)
                for g in range(2):
                    last = pe.transpose(ps_turn[:, g * P:(g + 1) * P], t_gu[:, g, :], ident[:, :])
                last.then_inc(t_turned, 1)
                if not first:
                    down_lora(t - 1)
                weights(6)
                base(ps_gate[1], "gate", 1)
                pe.wait_ge(b_gu_ready, t + 1)
                pe.wait_ge(tT_ready, t + 1)
                lora(ps_gate[0], 0, 0)
                lora(ps_up[0], 1, 0).then_inc(section_done, 1)
                if not first:
                    mix(t - 1)
                weights(8)
                base(ps_up[1], "up", 1)
                turn_act(t, 0)
                lora(ps_gate[1], 0, 1)
                lora(ps_up[1], 1, 1).then_inc(section_done, 1)
                weights(10)
                base(ps_gate[0], "gate", 2)
                weights(12)
                base(ps_up[0], "up", 2).then_inc(xT_used, 1)
                turn_act(t, 1)
                lora(ps_gate[0], 0, 2)
                lora(ps_up[0], 1, 2).then_inc(section_done, 1)
                pe.wait_ge(a_dn_ready, t + 1)
                weights(14)
                down_chunks(t, 0, 4)
                turn_act(t, 2)
                weights(len(PIECES))
                down_chunks(t, 4, NC).then_inc(down_done, 1)

            pe.wait_ge(ident_ready, 1)
            tile(0, first=True)
            with pe.Fori(1, TILES) as t:
                tile(t)
            turn_td(TILES - 1)
            down_lora(TILES - 1)
            mix(TILES - 1)


def kernel(x, itok_B_2_6, itok_B_0_15, L0_cond_W_gate, L0_cond_W_up, L0_cond_W_down, L0_cond_A_gate,
           L0_cond_B_gate, L0_cond_A_up, L0_cond_B_up, L0_cond_A_down, L0_cond_B_down, L1_cond_weights):
    import numpy as np
    import concourse.bacc as bacc
    from concourse.bass_utils import run_bass_kernel_spmd

    x = np.asarray(x)
    rows = x.reshape(SEQS * CH, H)

    def by_section(w):
        w = np.asarray(w).T.reshape(KH, P, F)
        return np.concatenate([w[:, :, c:c + n].transpose(1, 0, 2).reshape(P, KH * n) for c, n in SECTIONS], axis=1)

    def a_by_feature(a):
        return np.asarray(a)[0].reshape(ADAPTERS, RANK, KH, P).transpose(0, 3, 2, 1)

    a_down = np.asarray(L0_cond_A_down)[0]
    a_down_padded = np.zeros((ADAPTERS, RANK, NC * P), a_down.dtype)
    a_down_padded[:, :, :F] = a_down
    a_rows = np.concatenate([
        np.stack([a_by_feature(L0_cond_A_gate), a_by_feature(L0_cond_A_up)], axis=3).reshape(ADAPTERS * P, A_GU),
        a_down_padded.reshape(ADAPTERS, RANK, NC, P).transpose(0, 3, 2, 1).reshape(ADAPTERS * P, NC * RANK),
    ], axis=1)
    b_rows = np.concatenate([
        np.asarray(b)[0].transpose(0, 2, 1).reshape(ADAPTERS * RANK, -1)
        for b in (L0_cond_B_gate, L0_cond_B_up, L0_cond_B_down)], axis=1)

    adapter = np.asarray(itok_B_2_6).astype(np.int32, copy=False).reshape(TILES, TILE_SEQS)
    cond = np.asarray(itok_B_0_15).astype(np.int32, copy=False).reshape(TILES, TILE_SEQS)
    which = np.concatenate([
        np.broadcast_to(adapter, (P, TILES, TILE_SEQS)),
        np.tile(adapter.repeat(RANK, axis=1).T, (P // RR, 1))[:, :, None],
        cond.repeat(CH, axis=1).T[:, :, None],
    ], axis=2)
    p = np.arange(P, dtype=np.int32)
    mult = np.tile(np.array([P] * TILE_SEQS + [RANK, CH], np.int32), (P, 1))
    lane = np.stack([p] * TILE_SEQS + [p % RANK, p % CH], axis=1)

    arrays = {
        "x": rows,
        "xT": rows.reshape(TILES, P, KH, P).transpose(0, 3, 2, 1).reshape(TILES * P, KH * P),
        "w_gate": by_section(L0_cond_W_gate),
        "w_up": by_section(L0_cond_W_up),
        "w_down": np.asarray(L0_cond_W_down).T,
        "a_rows": a_rows,
        "b_rows": b_rows,
        "mix_rows": np.asarray(L1_cond_weights).reshape(ADAPTERS * CH, CH),
        "which": which,
        "mult": mult,
        "lane": lane,
    }
    nc = bacc.Bacc("TRN2", target_bir_lowering=False, num_devices=1, dynamic_dma_scratch_size=4096)
    arrays = {f"in_{k}": np.ascontiguousarray(v) for k, v in arrays.items()}
    args = [nc.dram_tensor(k, v.shape, mybir.dt.from_np(v.dtype), kind="ExternalInput").ap()
            for k, v in arrays.items()]
    out = nc.dram_tensor("out", (SEQS * CH, H), F32, kind="ExternalOutput").ap()
    build(nc, *args, out)
    result = run_bass_kernel_spmd(nc, [arrays], core_ids=[0])
    return result.results[0]["out"].reshape(SEQS, CH, H)
```

```python
from contextlib import ExitStack

import concourse.bass as bass
from concourse import mybir

F32 = mybir.dt.float32
F32R = mybir.dt.float32r
I32 = mybir.dt.int32
ALU = mybir.AluOpType
ACT = mybir.ActivationFunctionType

P = 128
SEQS, CH, H = 64, 32, 512
F = 1376
ADAPTERS, RANK = 16, 16
LORA_SCALE = 0.5
TILE_SEQS = P // CH
TILES = SEQS // TILE_SEQS
KH = H // P
RR = TILE_SEQS * RANK
SECTIONS = [(0, F - 1024), (F - 1024, 512), (F - 512, 512)]
NS = len(SECTIONS)
SECTION_CHUNKS = [[(c, min(P, c0 + n - c)) for c in range(c0, c0 + n, P)] for c0, n in SECTIONS]
CHUNKS = [c for chunks in SECTION_CHUNKS for c in chunks]
FIRST_CHUNK = [sum(map(len, SECTION_CHUNKS[:s])) for s in range(NS + 1)]
SHORT = next(i for i, (_, n) in enumerate(CHUNKS) if n < P)
NC = len(CHUNKS)
TC = 2 * RR
A_GU = KH * 2 * RANK
A_ROW = A_GU + NC * RANK
B_ROW = 2 * F + H
WD = H + RR
HALF = WD // 2
HALVES = [slice(0, HALF), slice(HALF, H)]
PIECE = 1024
SLOTS = 4


def weight_pieces():
    pieces = [(m, s, k) for s in range(NS) for m in ("gate", "up") for k in range(0, KH, 2)]
    c = 0
    while c < NC:
        n = 1 if c == SHORT or c + 1 in (SHORT, NC) else 2
        pieces.append(("down", c, n))
        c += n
    return pieces


PIECES = weight_pieces()
GU_PIECES = sum(m != "down" for m, _, _ in PIECES)


def pieces_to(m, s, k):
    return PIECES.index((m, s, k - k % 2)) + 1


def pieces_to_chunk(c):
    return next(i for i, (m, at, n) in enumerate(PIECES) if m == "down" and at <= c < at + n) + 1


def build(nc, x, xT, w_gate, w_up, w_down, a_rows, b_rows, mix_rows, which, mult, lane, out):
    with ExitStack() as ctx:
        def sb(name, shape, dt=F32):
            return ctx.enter_context(nc.sbuf_tensor(name, shape, dt))

        def bank(name):
            return ctx.enter_context(nc.psum_tensor(name, [P, 512], F32))

        def sem(name):
            return ctx.enter_context(nc.semaphore(name))

        w_cols = {"gate": KH * (F + TC), "up": KH * F}
        w_hi = {m: sb(f"w_{m}_hi", [P, w_cols[m]], F32R) for m in ("gate", "up")}
        w_lo = {m: sb(f"w_{m}_lo", [P, w_cols[m]], F32R) for m in ("gate", "up")}
        wd_hi = sb("wd_hi", [P, NC, WD], F32R)
        wd_lo = sb("wd_lo", [P, NC, WD], F32R)
        landing = sb("landing", [P, SLOTS, PIECE])
        a_raw = sb("a_raw", [P, TILE_SEQS, A_ROW])
        b_raw = sb("b_raw", [RR, B_ROW])
        b_gu = sb("b_gu", [P, 2 * F], F32R)
        b_dn = sb("b_dn", [P, H], F32R)
        xT_raw = sb("xT_raw", [P, KH * P])
        xT_hi = sb("xT_hi", [P, KH * P], F32R)
        xT_lo = sb("xT_lo", [P, KH * P], F32R)
        x_sb = sb("x_sb", [P, H])
        out_sb = sb("out_sb", [P, H])
        t_gu = sb("t_gu", [P, 2, 2 * RR])
        t_dn = sb("t_dn", [P, 2 * RR])
        tT_hi = sb("tT_hi", [P, 2, P], F32R)
        tT_lo = sb("tT_lo", [P, 2, P], F32R)
        tdT_hi = sb("tdT_hi", [P, P], F32R)
        tdT_lo = sb("tdT_lo", [P, P], F32R)
        act = [sb(f"act{i}", [P, 512]) for i in range(2)]
        actT_hi = sb("actT_hi", [P, NC, P], F32R)
        actT_lo = sb("actT_lo", [P, NC, P], F32R)
        mix_raw = sb("mix_raw", [P, CH])
        mix_w = sb("mix_w", [P, P])
        ident = sb("ident", [P, P])
        mask = sb("mask", [P, RR])
        which_sb = sb("which_sb", [P, TILES, TILE_SEQS + 2], I32)
        mult_sb = sb("mult_sb", [P, TILE_SEQS + 2], I32)
        lane_sb = sb("lane_sb", [P, TILE_SEQS + 2], I32)
        scaled = sb("scaled", [P, TILES, TILE_SEQS + 2], I32)
        rows = sb("rows", [P, TILES, TILE_SEQS + 2], I32)
        waited = sb("waited", [1, 1], I32)
        rows_now = sb("rows_now", [P, TILE_SEQS + 1], I32)
        mix_rows_now = sb("mix_rows_now", [P, 1], I32)

        ps_gate = [bank(f"ps_gate{i}") for i in range(2)]
        ps_up = [bank(f"ps_up{i}") for i in range(2)]
        ps_down = [bank(f"ps_down{i}") for i in range(2)]
        ps_turn = bank("ps_turn")
        ps_misc = bank("ps_misc")

        last_mix = [ps_misc, ps_up[1]]

        w_landed = [sem(f"w_landed{i}") for i in range(SLOTS)]
        which_landed = sem("which_landed")
        xT_landed = sem("xT_landed")
        x_landed = sem("x_landed")
        a_landed = sem("a_landed")
        b_landed = sem("b_landed")
        mix_landed = sem("mix_landed")
        stored = sem("stored")
        ident_zeroed = sem("ident_zeroed")
        ident_ready = sem("ident_ready")
        mask_zeroed = sem("mask_zeroed")
        mask_ready = sem("mask_ready")
        scaled_ready = sem("scaled_ready")
        rows_ready = sem("rows_ready")
        rows_copied = sem("rows_copied")
        mix_rows_copied = sem("mix_rows_copied")
        w_hi_ready = sem("w_hi_ready")
        xT_hi_ready = sem("xT_hi_ready")
        a_gu_hi_ready = sem("a_gu_hi_ready")
        b_gu_hi_ready = sem("b_gu_hi_ready")
        a_dn_hi_ready = sem("a_dn_hi_ready")
        b_dn_hi_ready = sem("b_dn_hi_ready")
        tT_hi_ready = sem("tT_hi_ready")
        tdT_hi_ready = sem("tdT_hi_ready")
        silu_ready = sem("silu_ready")
        actT_hi_ready = sem("actT_hi_ready")
        w_ready = sem("w_ready")
        xT_ready = sem("xT_ready")
        a_gu_ready = sem("a_gu_ready")
        b_gu_ready = sem("b_gu_ready")
        a_dn_ready = sem("a_dn_ready")
        b_dn_ready = sem("b_dn_ready")
        t_gu_ready = sem("t_gu_ready")
        tT_ready = sem("tT_ready")
        t_dn_ready = sem("t_dn_ready")
        tdT_ready = sem("tdT_ready")
        act_ready = sem("act_ready")
        actT_ready = sem("actT_ready")
        mix_ready = sem("mix_ready")
        h_ready = sem("h_ready")
        out_ready = sem("out_ready")
        t_done = sem("t_done")
        xT_used = sem("xT_used")
        section_done = sem("section_done")
        t_turned = sem("t_turned")
        td_turned = sem("td_turned")
        act_turned = sem("act_turned")
        down_done = sem("down_done")
        down_lora_done = sem("down_lora_done")
        mix_done = sem("mix_done")

        def w_at(w, m, s, k, ks=1, with_a=False):
            c0, n = SECTIONS[s]
            extra = TC if m == "gate" else 0
            step = n + (extra if s == 0 else 0)
            at = KH * (c0 + (extra if s else 0)) + k * step
            part = w[:, at:at + ks * step].rearrange("p (k c) -> p k c", c=step)
            return part if with_a else part[:, :, 0:n]

        def a_part(w):
            n = SECTIONS[0][1]
            return w_at(w, "gate", 0, 0, KH, with_a=True)[:, :, n:n + TC].rearrange("p k (q c) -> p q k c", q=TILE_SEQS)

        t_ps = slice(SECTIONS[0][1], SECTIONS[0][1] + TC)

        def slot_view(n):
            m, at, k = PIECES[n]
            slot = landing[:, n % SLOTS, :]
            if m == "down":
                rows_, cols = CHUNKS[at][1], k
                return (slot[0:rows_, 0:cols * H].rearrange("p (c n) -> p c n", n=H),
                        lambda part: {"hi": wd_hi, "lo": wd_lo}[part][0:rows_, at:at + cols, 0:H])
            return (slot[:, 0:2 * SECTIONS[at][1]].rearrange("p (k c) -> p k c", k=2),
                    lambda part: w_at({"hi": w_hi, "lo": w_lo}[part][m], m, at, k, 2))

        def turned(s):
            c, sizes = FIRST_CHUNK[s], [n for _, n in SECTION_CHUNKS[s]]
            whole = sizes.count(P)
            parts = [(P, c, whole, ps_turn[:, 0:whole * P].rearrange("p (c n) -> p c n", n=P))]
            if whole < len(sizes):
                parts.append((sizes[-1], c + whole, 1, ps_turn[0:sizes[-1], whole * P:(whole + 1) * P]
                              .rearrange("p (c n) -> p c n", n=P)))
            return parts

        block = ctx.enter_context(nc.Block())

        @block.sync
        def _(sp):
            def load_xT(t):
                sp.dma_start(xT_raw[:, :], xT[bass.ds(t * P, P), :]).then_inc(xT_landed, 16)

            def load_x(t):
                sp.dma_start(x_sb[:, :], x[bass.ds(t * P, P), :]).then_inc(x_landed, 16)

            def store(t):
                sp.wait_ge(out_ready, t + 1)
                sp.dma_start(out[bass.ds(t * P, P), :], out_sb[:, :]).then_inc(stored, 16)

            sp.dma_start(which_sb[:, :, :], which).then_inc(which_landed, 16)
            sp.dma_start(mult_sb[:, :], mult).then_inc(which_landed, 16)
            sp.dma_start(lane_sb[:, :], lane).then_inc(which_landed, 16)
            load_xT(0)
            for n, (m, at, k) in enumerate(PIECES):
                if n == GU_PIECES:
                    sp.wait_ge(xT_ready, 1)
                    load_xT(1)
                    load_x(0)
                if n >= SLOTS:
                    sp.wait_ge(w_ready, n - SLOTS + 1)
                raw, _ = slot_view(n)
                if m == "down":
                    f0, rows_ = CHUNKS[at]
                    src = w_down[f0:f0 + k * rows_, :].rearrange("(c p) n -> p c n", p=rows_)
                else:
                    c0, cols = SECTIONS[at]
                    src = {"gate": w_gate, "up": w_up}[m][:, KH * c0 + k * cols:KH * c0 + (k + 2) * cols]\
                        .rearrange("p (k c) -> p k c", k=2)
                sp.dma_start(raw, src).then_inc(w_landed[n % SLOTS], 16)
            with sp.Fori(2, TILES) as t:
                sp.wait_ge(xT_ready, t)
                load_xT(t)
                store(t - 2)
                load_x(t - 1)
            store(TILES - 2)
            load_x(TILES - 1)
            for half, cols in enumerate(HALVES):
                sp.wait_ge(out_ready, TILES + half)
                sp.dma_start(out[(TILES - 1) * P:TILES * P, cols], out_sb[:, cols]).then_inc(stored, 16)
            sp.wait_ge(stored, 16 * (TILES + 1))

        @block.gpsimd
        def _(pool):
            pool.memset(ident[:, :], 0.0).then_inc(ident_zeroed, 1)
            pool.wait_ge(ident_zeroed, 1)
            pool.affine_select(out=ident[:, :], in_=ident[:, :], compare_op=ALU.not_equal, fill=1.0, base=0,
                               pattern=[[-1, P]], channel_multiplier=1).then_inc(ident_ready, 1)
            pool.wait_ge(rows_ready, 1)

            def indirect_after(semaphore, value):
                pool.wait_ge(semaphore, value)
                pool.tensor_tensor(waited[:, :], lane_sb[0:1, 0:1], lane_sb[0:1, 0:1], ALU.add)

            def gathers(t, first=False):
                if not first:
                    pool.wait_ge(a_dn_ready, t)
                    pool.wait_ge(b_dn_ready, t)
                now = rows[:, bass.ds(t, 1), :].rearrange("p o c -> p (o c)")
                pool.tensor_copy(rows_now[:, :], now[:, 0:TILE_SEQS + 1])\
                    .then_inc(rows_copied, 1)
                indirect_after(rows_copied, t + 1)
                for q in range(TILE_SEQS):
                    pool.indirect_dma_start(
                        a_raw[:, q, :], None, a_rows,
                        bass.IndirectOffsetOnAxis(ap=rows_now[:, q:q + 1], axis=0)).then_inc(a_landed, 16)
                pool.indirect_dma_start(
                    b_raw[:, :], None, b_rows,
                    bass.IndirectOffsetOnAxis(ap=rows_now[0:RR, TILE_SEQS:TILE_SEQS + 1], axis=0))\
                    .then_inc(b_landed, 16)
                if not first:
                    pool.wait_ge(mix_ready, t)
                pool.tensor_copy(mix_rows_now[:, :], now[:, TILE_SEQS + 1:TILE_SEQS + 2]).then_inc(mix_rows_copied, 1)
                indirect_after(mix_rows_copied, t + 1)
                pool.indirect_dma_start(
                    mix_raw[:, :], None, mix_rows,
                    bass.IndirectOffsetOnAxis(ap=mix_rows_now[:, :], axis=0))\
                    .then_inc(mix_landed, 16)

            gathers(0, first=True)
            with pool.Fori(1, TILES) as t:
                gathers(t)

        @block.scalar
        def _(sc):
            def hi(dst, src):
                return nc.scalar.activation(dst, src, ACT.Copy)

            def split_x(t, first=False):
                sc.wait_ge(xT_landed, 16 * (t + 1))
                if not first:
                    sc.wait_ge(xT_used, t)
                hi(xT_hi[:, :], xT_raw[:, :]).then_inc(xT_hi_ready, 1)

            def split_a_gu(t, first=False):
                sc.wait_ge(a_landed, 16 * TILE_SEQS * (t + 1))
                if not first:
                    sc.wait_ge(t_done, t)
                hi(a_part(w_hi["gate"]), a_raw[:, :, 0:A_GU].rearrange("p q (k c) -> p q k c", k=KH)).then_inc(a_gu_hi_ready, 1)

            def split_b_gu(t, first=False):
                sc.wait_ge(b_landed, 16 * (t + 1))
                if not first:
                    sc.wait_ge(section_done, NS * t)
                hi(b_gu[0:RR, :], b_raw[:, 0:2 * F]).then_inc(b_gu_hi_ready, 1)

            def split_weights(n0, n1):
                for n in range(n0, n1):
                    raw, to = slot_view(n)
                    sc.wait_ge(w_landed[n % SLOTS], 16 * (n // SLOTS + 1))
                    hi(to("hi"), raw).then_inc(w_hi_ready, 1)

            def turn_td(t):
                sc.wait_ge(td_turned, t + 1)
                hi(tdT_hi[:, :], ps_turn[:, 0:P]).then_inc(tdT_hi_ready, 1)

            def silu(t, s):
                n = SECTIONS[s][1]
                sc.wait_ge(section_done, NS * t + s + 1)
                if s == 2:
                    sc.wait_ge(act_turned, NS * t + 1)
                nc.scalar.activation(act[s % 2][:, 0:n], ps_gate[s % 2][:, 0:n], ACT.Silu).then_inc(silu_ready, 1)

            def act_hi(t, s):
                sc.wait_ge(act_turned, NS * t + s + 1)
                for rows_, c, cols, src in turned(s):
                    i = hi(actT_hi[0:rows_, c:c + cols, :], src)
                i.then_inc(actT_hi_ready, 1)

            def adapters_down(t, first):
                hi(wd_hi[:, :, H:WD].rearrange("p c (q r) -> p q c r", q=TILE_SEQS),
                   a_raw[:, :, A_GU:A_ROW].rearrange("p q (c r) -> p q c r", c=NC)).then_inc(a_dn_hi_ready, 1)
                if not first:
                    sc.wait_ge(down_lora_done, 2 * t)
                hi(b_dn[0:RR, :], b_raw[:, 2 * F:B_ROW]).then_inc(b_dn_hi_ready, 1)

            def tile(t, first=False, last=False):
                if first:
                    split_x(t, first)
                    split_weights(0, 2)
                    split_a_gu(t, first)
                    split_weights(2, 6)
                else:
                    turn_td(t - 1)
                if first:
                    split_b_gu(t, first)
                sc.wait_ge(t_turned, t + 1)
                hi(tT_hi[:, :, :], ps_turn[:, 0:2 * P].rearrange("p (g n) -> p g n", g=2)).then_inc(tT_hi_ready, 1)
                if first:
                    split_weights(6, 8)
                else:
                    adapters_down(t, first)
                silu(t, 0)
                if first:
                    split_weights(8, 10)
                act_hi(t, 0)
                if first:
                    split_weights(10, 12)
                    adapters_down(t, first)
                silu(t, 1)
                if first:
                    split_weights(12, 14)
                act_hi(t, 1)
                if not last:
                    split_x(t + 1)
                if first:
                    split_weights(14, 16)
                silu(t, 2)
                if first:
                    split_weights(16, len(PIECES))
                act_hi(t, 2)
                if not last:
                    split_a_gu(t + 1)
                    split_b_gu(t + 1)

            tile(0, first=True)
            with sc.Fori(1, TILES - 1) as t:
                tile(t)
            tile(TILES - 1, last=True)
            turn_td(TILES - 1)

        @block.vector
        def _(ve):
            def lo(dst, src, hi_part):
                return nc.vector.tensor_tensor(dst, src, hi_part.bitcast(F32), ALU.subtract)

            def split_x(t):
                ve.wait_ge(xT_hi_ready, t + 1)
                lo(xT_lo[:, :], xT_raw[:, :], xT_hi[:, :]).then_inc(xT_ready, 1)

            def split_a_gu(t):
                ve.wait_ge(a_gu_hi_ready, t + 1)
                lo(a_part(w_lo["gate"]), a_raw[:, :, 0:A_GU].rearrange("p q (k c) -> p q k c", k=KH),
                   a_part(w_hi["gate"])).then_inc(a_gu_ready, 1)

            def split_b_gu(t):
                ve.wait_ge(b_gu_hi_ready, t + 1)
                lo(b_gu[RR:2 * RR, :], b_raw[:, 0:2 * F], b_gu[0:RR, :]).then_inc(b_gu_ready, 1)

            def split_weights(n0, n1):
                for n in range(n0, n1):
                    raw, to = slot_view(n)
                    ve.wait_ge(w_hi_ready, n + 1)
                    lo(to("lo"), raw, to("hi")).then_inc(w_ready, 1)

            def twice(ap, lead):
                o = ap.rearrange("p (o q r) -> p o q r", o=1, q=TILE_SEQS) if lead is None else lead
                return o.to_broadcast([P, 2, TILE_SEQS, RANK])

            mask2 = twice(mask[:, :], None)

            def mask_td(t):
                ve.wait_ge(down_done, t + 1)
                nc.vector.tensor_tensor(
                    t_dn[:, :].rearrange("p (o q r) -> p o q r", o=2, q=TILE_SEQS),
                    twice(ps_down[1][:, HALF - RR:HALF], None), mask2, ALU.mult).then_inc(t_dn_ready, 1)

            def mask_t(t):
                ve.wait_ge(t_done, t + 1)
                by_seq = ps_gate[0][:, t_ps].rearrange("p (o q g r) -> p o q g r", o=1, q=TILE_SEQS, g=2)
                for g in range(2):
                    last = nc.vector.tensor_tensor(
                        t_gu[:, g, :].rearrange("p (o q r) -> p o q r", o=2, q=TILE_SEQS),
                        twice(None, by_seq[:, :, :, g, :]), mask2, ALU.mult)
                last.then_inc(t_gu_ready, 1)

            def turn_td(t):
                ve.wait_ge(tdT_hi_ready, t + 1)
                lo(tdT_lo[:, :], ps_turn[:, 0:P], tdT_hi[:, :]).then_inc(tdT_ready, 1)

            def turn_t(t):
                ve.wait_ge(tT_hi_ready, t + 1)
                lo(tT_lo[:, :, :], ps_turn[:, 0:2 * P].rearrange("p (g n) -> p g n", g=2), tT_hi[:, :, :])\
                    .then_inc(tT_ready, 1)

            def spread_mix(t):
                ve.wait_ge(mix_landed, 16 * (t + 1))
                for q in range(TILE_SEQS):
                    r = slice(q * CH, (q + 1) * CH)
                    last = nc.vector.tensor_copy(mix_w[r, r], mix_raw[r, :])
                last.then_inc(mix_ready, 1)

            def residual_h(t):
                ve.wait_ge(x_landed, 16 * (t + 1))
                for half, cols in enumerate(HALVES):
                    ve.wait_ge(down_lora_done, 2 * t + half + 1)
                    nc.vector.tensor_tensor(x_sb[:, cols], x_sb[:, cols], ps_down[half][:, 0:cols.stop - cols.start],
                                            ALU.add).then_inc(h_ready, 1)

            def residual_out(t, first=False):
                ve.wait_ge(mix_done, 2 * (t + 1))
                if not first:
                    ve.wait_ge(stored, 16 * t)
                nc.vector.tensor_tensor(out_sb[:, :], x_sb[:, :], ps_misc[:, 0:H], ALU.add).then_inc(out_ready, 1)

            def gating(t, s):
                n = SECTIONS[s][1]
                ve.wait_ge(silu_ready, NS * t + s + 1)
                nc.vector.tensor_tensor(act[s % 2][:, 0:n], act[s % 2][:, 0:n], ps_up[s % 2][:, 0:n], ALU.mult)\
                    .then_inc(act_ready, 1)

            def act_lo(t, s):
                ve.wait_ge(actT_hi_ready, NS * t + s + 1)
                for rows_, c, cols, src in turned(s):
                    i = lo(actT_lo[0:rows_, c:c + cols, :], src, actT_hi[0:rows_, c:c + cols, :])
                i.then_inc(actT_ready, 1)

            def adapters_down(t):
                ve.wait_ge(a_dn_hi_ready, t + 1)
                lo(wd_lo[:, :, H:WD].rearrange("p c (q r) -> p q c r", q=TILE_SEQS),
                   a_raw[:, :, A_GU:A_ROW].rearrange("p q (c r) -> p q c r", c=NC),
                   wd_hi[:, :, H:WD].rearrange("p c (q r) -> p q c r", q=TILE_SEQS)).then_inc(a_dn_ready, 1)
                ve.wait_ge(b_dn_hi_ready, t + 1)
                lo(b_dn[RR:2 * RR, :], b_raw[:, 2 * F:B_ROW], b_dn[0:RR, :]).then_inc(b_dn_ready, 1)

            def tile(t, first=False, last=False):
                if first:
                    split_x(t)
                    split_weights(0, 2)
                    split_a_gu(t)
                    split_weights(2, 6)
                else:
                    mask_td(t - 1)
                mask_t(t)
                if first:
                    split_b_gu(t)
                else:
                    turn_td(t - 1)
                turn_t(t)
                if first:
                    split_weights(6, 8)
                else:
                    spread_mix(t - 1)
                    residual_h(t - 1)
                    adapters_down(t)
                gating(t, 0)
                if first:
                    split_weights(8, 10)
                else:
                    residual_out(t - 1, first=isinstance(t, int) and t == 1)
                act_lo(t, 0)
                if first:
                    split_weights(10, 12)
                    adapters_down(t)
                gating(t, 1)
                if first:
                    split_weights(12, 14)
                act_lo(t, 1)
                if not last:
                    split_x(t + 1)
                if first:
                    split_weights(14, 16)
                gating(t, 2)
                if first:
                    split_weights(16, len(PIECES))
                act_lo(t, 2)
                if not last:
                    split_a_gu(t + 1)
                    split_b_gu(t + 1)

            nc.vector.memset(mix_w[:, :], 0.0).then_inc(mask_zeroed, 1)
            nc.vector.memset(mask[:, :], 0.0).then_inc(mask_zeroed, 1)
            ve.wait_ge(mask_zeroed, 2)
            for q in range(TILE_SEQS):
                last = nc.vector.memset(mask[q * CH:(q + 1) * CH, q * RANK:(q + 1) * RANK], LORA_SCALE)
            last.then_inc(mask_ready, 1)
            ve.wait_ge(which_landed, 48)
            each = [P, TILES, TILE_SEQS + 2]
            nc.vector.tensor_tensor(scaled[:, :, :], which_sb[:, :, :],
                                    mult_sb[:, :].rearrange("p (o c) -> p o c", o=1).to_broadcast(each),
                                    ALU.mult).then_inc(scaled_ready, 1)
            ve.wait_ge(scaled_ready, 1)
            nc.vector.tensor_tensor(rows[:, :, :], scaled[:, :, :],
                                    lane_sb[:, :].rearrange("p (o c) -> p o c", o=1).to_broadcast(each),
                                    ALU.add).then_inc(rows_ready, 1)

            ve.wait_ge(mask_ready, 1)
            tile(0, first=True)
            tile(1)
            with ve.Fori(2, TILES - 1) as t:
                tile(t)
            tile(TILES - 1, last=True)
            mask_td(TILES - 1)
            turn_td(TILES - 1)
            spread_mix(TILES - 1)
            residual_h(TILES - 1)
            ve.wait_ge(stored, 16 * (TILES - 1))
            for half, cols in enumerate(HALVES):
                ve.wait_ge(mix_done, 2 * (TILES - 1) + half + 1)
                nc.vector.tensor_tensor(out_sb[:, cols], x_sb[:, cols],
                                        last_mix[half][:, 0:cols.stop - cols.start], ALU.add).then_inc(out_ready, 1)

        @block.tensor
        def _(pe):
            def base(ps, m, s, first=False, columns=None):
                with_a = m == "gate" and s == 0
                cols = columns or slice(0, SECTIONS[s][1] + (TC if with_a and not first else 0))
                stops = not (first and with_a and not columns)
                for k in range(KH):
                    if first and not columns and k % 2 == 0:
                        pe.wait_ge(w_ready, pieces_to(m, s, k))
                    x_hi, x_lo = xT_hi[:, k * P:(k + 1) * P], xT_lo[:, k * P:(k + 1) * P]
                    hi, lo = (w_at(w[m], m, s, k, with_a=True)[:, 0, cols] for w in (w_hi, w_lo))
                    pe.matmul(ps[:, cols], x_hi, hi, start=(k == 0 and not columns), stop=False)
                    pe.matmul(ps[:, cols], x_hi, lo, start=False, stop=False)
                    last = pe.matmul(ps[:, cols], x_lo, hi, start=False, stop=stops and k == KH - 1)
                return last

            def lora(ps, g, s):
                c0, n = SECTIONS[s]
                b = b_gu[:, g * F + c0:g * F + c0 + n]
                pe.matmul(ps[:, 0:n], tT_hi[:, g, :], b, start=False, stop=False, skip_group_check=True)
                return pe.matmul(ps[:, 0:n], tT_lo[:, g, :], b, start=False, stop=True, skip_group_check=True)

            def turn_act(t, s):
                pe.wait_ge(act_ready, NS * t + s + 1)
                if s == 0:
                    pe.wait_ge(tT_ready, t + 1)
                else:
                    pe.wait_ge(actT_ready, NS * t + s)
                for i, (f0, n) in enumerate(SECTION_CHUNKS[s]):
                    at = f0 - SECTIONS[s][0]
                    last = pe.transpose(ps_turn[0:n, i * P:(i + 1) * P], act[s % 2][:, at:at + n], ident[:, :])
                last.then_inc(act_turned, 1)

            def down_chunks(t, s, first=False):
                pe.wait_ge(actT_ready, NS * t + s + 1)
                for c in range(FIRST_CHUNK[s], FIRST_CHUNK[s + 1]):
                    if first:
                        pe.wait_ge(w_ready, pieces_to_chunk(c))
                    k = CHUNKS[c][1]
                    for a, w in ((actT_hi, wd_hi), (actT_hi, wd_lo), (actT_lo, wd_hi)):
                        for half in range(2):
                            last = pe.matmul(ps_down[half][:, 0:HALF], a[0:k, c, :],
                                             w[0:k, c, half * HALF:(half + 1) * HALF],
                                             start=(c == 0 and a is actT_hi and w is wd_hi),
                                             stop=(c == NC - 1 and a is actT_lo))
                return last

            def turn_td(t):
                pe.wait_ge(t_dn_ready, t + 1)
                pe.wait_ge(actT_ready, NS * (t + 1))
                pe.transpose(ps_turn[:, 0:P], t_dn[:, :], ident[:, :]).then_inc(td_turned, 1)

            def down_lora(t):
                pe.wait_ge(tdT_ready, t + 1)
                for half, cols in enumerate(HALVES):
                    for td in (tdT_hi, tdT_lo):
                        last = pe.matmul(ps_down[half][:, 0:cols.stop - cols.start], td[:, :], b_dn[:, cols],
                                         start=False, stop=(td is tdT_lo), skip_group_check=True)
                    last.then_inc(down_lora_done, 1)

            def mix(t, banks):
                pe.wait_ge(mix_ready, t + 1)
                for half, cols in enumerate(HALVES):
                    pe.wait_ge(h_ready, 2 * t + half + 1)
                    at = cols if banks[half] is ps_misc else slice(0, cols.stop - cols.start)
                    pe.matmul(banks[half][:, at], mix_w[:, :], x_sb[:, cols], start=True, stop=True)\
                      .then_inc(mix_done, 1)

            def tile(t, first=False):
                pe.wait_ge(xT_ready, t + 1)
                if not first:
                    pe.wait_ge(a_gu_ready, t + 1)
                    pe.wait_ge(act_ready, NS * t)
                gate = base(ps_gate[0], "gate", 0, first)
                if first:
                    pe.wait_ge(a_gu_ready, 1)
                    gate = base(ps_gate[0], "gate", 0, first, columns=t_ps)
                gate.then_inc(t_done, 1)
                if not first:
                    turn_td(t - 1)
                base(ps_up[0], "up", 0, first)
                pe.wait_ge(t_gu_ready, t + 1)
                if not first:
                    pe.wait_ge(tdT_ready, t)
                for g in range(2):
                    last = pe.transpose(ps_turn[:, g * P:(g + 1) * P], t_gu[:, g, :], ident[:, :])
                last.then_inc(t_turned, 1)
                if not first:
                    down_lora(t - 1)
                base(ps_gate[1], "gate", 1, first)
                pe.wait_ge(b_gu_ready, t + 1)
                pe.wait_ge(tT_ready, t + 1)
                lora(ps_gate[0], 0, 0)
                lora(ps_up[0], 1, 0).then_inc(section_done, 1)
                if not first:
                    mix(t - 1, [ps_misc, ps_misc])
                base(ps_up[1], "up", 1, first)
                turn_act(t, 0)
                lora(ps_gate[1], 0, 1)
                lora(ps_up[1], 1, 1).then_inc(section_done, 1)
                base(ps_gate[0], "gate", 2, first)
                base(ps_up[0], "up", 2, first).then_inc(xT_used, 1)
                turn_act(t, 1)
                lora(ps_gate[0], 0, 2)
                lora(ps_up[0], 1, 2).then_inc(section_done, 1)
                pe.wait_ge(a_dn_ready, t + 1)
                down_chunks(t, 0, first)
                turn_act(t, 2)
                down_chunks(t, 1, first)
                down_chunks(t, 2, first).then_inc(down_done, 1)

            pe.wait_ge(ident_ready, 1)
            tile(0, first=True)
            with pe.Fori(1, TILES) as t:
                tile(t)
            turn_td(TILES - 1)
            down_lora(TILES - 1)
            mix(TILES - 1, last_mix)


def kernel(x, itok_B_2_6, itok_B_0_15, L0_cond_W_gate, L0_cond_W_up, L0_cond_W_down, L0_cond_A_gate,
           L0_cond_B_gate, L0_cond_A_up, L0_cond_B_up, L0_cond_A_down, L0_cond_B_down, L1_cond_weights):
    import numpy as np
    import concourse.bacc as bacc
    from concourse.bass_utils import run_bass_kernel_spmd

    x = np.asarray(x)
    rows = x.reshape(SEQS * CH, H)

    def by_section(w):
        w = np.asarray(w).T.reshape(KH, P, F)
        return np.concatenate([w[:, :, c:c + n].transpose(1, 0, 2).reshape(P, KH * n) for c, n in SECTIONS], axis=1)

    def a_by_feature(a):
        return np.asarray(a)[0].reshape(ADAPTERS, RANK, KH, P).transpose(0, 3, 2, 1)

    a_down = np.asarray(L0_cond_A_down)[0]
    a_down_padded = np.zeros((ADAPTERS, RANK, NC, P), a_down.dtype)
    for c, (f0, n) in enumerate(CHUNKS):
        a_down_padded[:, :, c, :n] = a_down[:, :, f0:f0 + n]
    a_rows = np.concatenate([
        np.stack([a_by_feature(L0_cond_A_gate), a_by_feature(L0_cond_A_up)], axis=3).reshape(ADAPTERS * P, A_GU),
        a_down_padded.transpose(0, 3, 2, 1).reshape(ADAPTERS * P, NC * RANK),
    ], axis=1)
    b_rows = np.concatenate([
        np.asarray(b)[0].transpose(0, 2, 1).reshape(ADAPTERS * RANK, -1)
        for b in (L0_cond_B_gate, L0_cond_B_up, L0_cond_B_down)], axis=1)

    adapter = np.asarray(itok_B_2_6).astype(np.int32, copy=False).reshape(TILES, TILE_SEQS)
    cond = np.asarray(itok_B_0_15).astype(np.int32, copy=False).reshape(TILES, TILE_SEQS)
    which = np.concatenate([
        np.broadcast_to(adapter, (P, TILES, TILE_SEQS)),
        np.tile(adapter.repeat(RANK, axis=1).T, (P // RR, 1))[:, :, None],
        cond.repeat(CH, axis=1).T[:, :, None],
    ], axis=2)
    p = np.arange(P, dtype=np.int32)
    mult = np.tile(np.array([P] * TILE_SEQS + [RANK, CH], np.int32), (P, 1))
    lane = np.stack([p] * TILE_SEQS + [p % RANK, p % CH], axis=1)

    arrays = {
        "x": rows,
        "xT": rows.reshape(TILES, P, KH, P).transpose(0, 3, 2, 1).reshape(TILES * P, KH * P),
        "w_gate": by_section(L0_cond_W_gate),
        "w_up": by_section(L0_cond_W_up),
        "w_down": np.asarray(L0_cond_W_down).T,
        "a_rows": a_rows,
        "b_rows": b_rows,
        "mix_rows": np.asarray(L1_cond_weights).reshape(ADAPTERS * CH, CH),
        "which": which,
        "mult": mult,
        "lane": lane,
    }
    nc = bacc.Bacc("TRN2", target_bir_lowering=False, num_devices=1, dynamic_dma_scratch_size=4096)
    arrays = {f"in_{k}": np.ascontiguousarray(v) for k, v in arrays.items()}
    args = [nc.dram_tensor(k, v.shape, mybir.dt.from_np(v.dtype), kind="ExternalInput").ap()
            for k, v in arrays.items()]
    out = nc.dram_tensor("out", (SEQS * CH, H), F32, kind="ExternalOutput").ap()
    build(nc, *args, out)
    result = run_bass_kernel_spmd(nc, [arrays], core_ids=[0])
    return result.results[0]["out"].reshape(SEQS, CH, H)
```
